# Optimizing a Trainium2 kernel written in Bass

```python
import numpy as np
import jax
import jax.numpy as jnp

def _softmax(x, axis=-1):
    return jax.nn.softmax(x, axis=axis)

def _gelu(x):
    return jax.nn.gelu(x, approximate=True)

def _silu(x):
    return jax.nn.silu(x)

def _sigmoid(x):
    return jax.nn.sigmoid(x)

def _layernorm(x, axis=-1, eps=1e-05):
    m = jnp.mean(x, axis=axis, keepdims=True)
    v = jnp.var(x, axis=axis, keepdims=True)
    return (x - m) / jnp.sqrt(v + eps)

def _scatter_add(tgt, idx, src, axis=0):
    return tgt.at[idx].add(src)

def _segment_sum(src, seg, n):
    return jax.ops.segment_sum(src, seg, n)
kernel_name = 'mk_dlrm_tower_d1_rec_r8_eea472'

def setup_inputs(seed: int=0):
    np.random.seed(seed)
    _w = jnp.asarray

    def _rec_inputs():
        import jax
        import jax.numpy as jnp
        _tk = jax.random.key(seed)
        ids = jnp.stack([jax.random.randint(jax.random.fold_in(_tk, 200 + f), (512,), 0, v, jnp.int32) for f, v in enumerate([125000, 1000, 1000, 1000, 1250, 1000, 12500, 1000, 12500, 1250, 1250, 1250, 12500, 12500, 12500, 12500, 1000, 1250, 1000, 1000, 1000, 12500, 1000, 12500, 1250, 1250])], axis=1)
        tbl_0 = 0.05 * jax.random.normal(jax.random.fold_in(_tk, 500 + 0), (125000, 128), jnp.float32)
        tbl_1 = 0.05 * jax.random.normal(jax.random.fold_in(_tk, 500 + 1), (1000, 128), jnp.float32)
        tbl_2 = 0.05 * jax.random.normal(jax.random.fold_in(_tk, 500 + 2), (1000, 128), jnp.float32)
        tbl_3 = 0.05 * jax.random.normal(jax.random.fold_in(_tk, 500 + 3), (1000, 128), jnp.float32)
        tbl_4 = 0.05 * jax.random.normal(jax.random.fold_in(_tk, 500 + 4), (1250, 128), jnp.float32)
        tbl_5 = 0.05 * jax.random.normal(jax.random.fold_in(_tk, 500 + 5), (1000, 128), jnp.float32)
        tbl_6 = 0.05 * jax.random.normal(jax.random.fold_in(_tk, 500 + 6), (12500, 128), jnp.float32)
        tbl_7 = 0.05 * jax.random.normal(jax.random.fold_in(_tk, 500 + 7), (1000, 128), jnp.float32)
        tbl_8 = 0.05 * jax.random.normal(jax.random.fold_in(_tk, 500 + 8), (12500, 128), jnp.float32)
        tbl_9 = 0.05 * jax.random.normal(jax.random.fold_in(_tk, 500 + 9), (1250, 128), jnp.float32)
        tbl_10 = 0.05 * jax.random.normal(jax.random.fold_in(_tk, 500 + 10), (1250, 128), jnp.float32)
        tbl_11 = 0.05 * jax.random.normal(jax.random.fold_in(_tk, 500 + 11), (1250, 128), jnp.float32)
        tbl_12 = 0.05 * jax.random.normal(jax.random.fold_in(_tk, 500 + 12), (12500, 128), jnp.float32)
        tbl_13 = 0.05 * jax.random.normal(jax.random.fold_in(_tk, 500 + 13), (12500, 128), jnp.float32)
        tbl_14 = 0.05 * jax.random.normal(jax.random.fold_in(_tk, 500 + 14), (12500, 128), jnp.float32)
        tbl_15 = 0.05 * jax.random.normal(jax.random.fold_in(_tk, 500 + 15), (12500, 128), jnp.float32)
        tbl_16 = 0.05 * jax.random.normal(jax.random.fold_in(_tk, 500 + 16), (1000, 128), jnp.float32)
        tbl_17 = 0.05 * jax.random.normal(jax.random.fold_in(_tk, 500 + 17), (1250, 128), jnp.float32)
        tbl_18 = 0.05 * jax.random.normal(jax.random.fold_in(_tk, 500 + 18), (1000, 128), jnp.float32)
        tbl_19 = 0.05 * jax.random.normal(jax.random.fold_in(_tk, 500 + 19), (1000, 128), jnp.float32)
        tbl_20 = 0.05 * jax.random.normal(jax.random.fold_in(_tk, 500 + 20), (1000, 128), jnp.float32)
        tbl_21 = 0.05 * jax.random.normal(jax.random.fold_in(_tk, 500 + 21), (12500, 128), jnp.float32)
        tbl_22 = 0.05 * jax.random.normal(jax.random.fold_in(_tk, 500 + 22), (1000, 128), jnp.float32)
        tbl_23 = 0.05 * jax.random.normal(jax.random.fold_in(_tk, 500 + 23), (12500, 128), jnp.float32)
        tbl_24 = 0.05 * jax.random.normal(jax.random.fold_in(_tk, 500 + 24), (1250, 128), jnp.float32)
        tbl_25 = 0.05 * jax.random.normal(jax.random.fold_in(_tk, 500 + 25), (1250, 128), jnp.float32)
        _rk = jax.random.fold_in(_tk, 7)
        r_bottom_output = -0.000520686 + 1.00062 * jax.random.normal(jax.random.fold_in(_rk, 101), (512, 128), jnp.float32)
        W_top1 = 0.0456912 * jax.random.normal(jax.random.fold_in(_tk, 801), (479, 512), jnp.float32)
        W_top2 = 0.0441942 * jax.random.normal(jax.random.fold_in(_tk, 802), (512, 256), jnp.float32)
        W_top3 = 0.0625 * jax.random.normal(jax.random.fold_in(_tk, 803), (256, 1), jnp.float32)
        b_top1 = jnp.zeros((512,), jnp.float32)
        b_top2 = jnp.zeros((256,), jnp.float32)
        return (r_bottom_output, ids, tbl_0, tbl_1, tbl_2, tbl_3, tbl_4, tbl_5, tbl_6, tbl_7, tbl_8, tbl_9, tbl_10, tbl_11, tbl_12, tbl_13, tbl_14, tbl_15, tbl_16, tbl_17, tbl_18, tbl_19, tbl_20, tbl_21, tbl_22, tbl_23, tbl_24, tbl_25, W_top1, b_top1, W_top2, b_top2, W_top3)
    r_bottom_output, ids, tbl_0, tbl_1, tbl_2, tbl_3, tbl_4, tbl_5, tbl_6, tbl_7, tbl_8, tbl_9, tbl_10, tbl_11, tbl_12, tbl_13, tbl_14, tbl_15, tbl_16, tbl_17, tbl_18, tbl_19, tbl_20, tbl_21, tbl_22, tbl_23, tbl_24, tbl_25, W_top1, b_top1, W_top2, b_top2, W_top3 = _rec_inputs()

    def _L0_rec_setup():
        import jax, jax.numpy as jnp
        import numpy as np
        NUM_FEATURES = 27
        _TRIU_I, _TRIU_J = np.triu_indices(NUM_FEATURES, k=1)
        key = jax.random.key(seed)
        k1, k2 = jax.random.split(key)
        bottom_output = jax.random.normal(k1, (2048, 128), dtype=jnp.float32)
        embeddings = jax.random.normal(k2, (2048, 26, 128), dtype=jnp.float32)
        return {'bottom_output': bottom_output, 'embeddings': embeddings}
    _L0_rec_all = _L0_rec_setup()
    _L0_rec_in = {k: v for k, v in _L0_rec_all.items() if k in ()}
    del _L0_rec_all
    return {'r_bottom_output': r_bottom_output, 'ids': ids, 'tbl_0': tbl_0, 'tbl_1': tbl_1, 'tbl_2': tbl_2, 'tbl_3': tbl_3, 'tbl_4': tbl_4, 'tbl_5': tbl_5, 'tbl_6': tbl_6, 'tbl_7': tbl_7, 'tbl_8': tbl_8, 'tbl_9': tbl_9, 'tbl_10': tbl_10, 'tbl_11': tbl_11, 'tbl_12': tbl_12, 'tbl_13': tbl_13, 'tbl_14': tbl_14, 'tbl_15': tbl_15, 'tbl_16': tbl_16, 'tbl_17': tbl_17, 'tbl_18': tbl_18, 'tbl_19': tbl_19, 'tbl_20': tbl_20, 'tbl_21': tbl_21, 'tbl_22': tbl_22, 'tbl_23': tbl_23, 'tbl_24': tbl_24, 'tbl_25': tbl_25, 'W_top1': W_top1, 'b_top1': b_top1, 'W_top2': W_top2, 'b_top2': b_top2, 'W_top3': W_top3}

def reference(r_bottom_output, ids, tbl_0, tbl_1, tbl_2, tbl_3, tbl_4, tbl_5, tbl_6, tbl_7, tbl_8, tbl_9, tbl_10, tbl_11, tbl_12, tbl_13, tbl_14, tbl_15, tbl_16, tbl_17, tbl_18, tbl_19, tbl_20, tbl_21, tbl_22, tbl_23, tbl_24, tbl_25, W_top1, b_top1, W_top2, b_top2, W_top3):
    import jax
    import jax.numpy as jnp

    def _L0_rec_ref(bottom_output, embeddings):
        import jax, jax.numpy as jnp
        import numpy as np
        NUM_FEATURES = 27
        _TRIU_I, _TRIU_J = np.triu_indices(NUM_FEATURES, k=1)
        all_emb = jnp.concatenate([bottom_output[:, None, :], embeddings], axis=1)
        gram = jnp.einsum('bfd,bgd->bfg', all_emb, all_emb)
        return gram[:, _TRIU_I, _TRIU_J]
    e = jnp.stack([tbl_0[ids[:, 0]], tbl_1[ids[:, 1]], tbl_2[ids[:, 2]], tbl_3[ids[:, 3]], tbl_4[ids[:, 4]], tbl_5[ids[:, 5]], tbl_6[ids[:, 6]], tbl_7[ids[:, 7]], tbl_8[ids[:, 8]], tbl_9[ids[:, 9]], tbl_10[ids[:, 10]], tbl_11[ids[:, 11]], tbl_12[ids[:, 12]], tbl_13[ids[:, 13]], tbl_14[ids[:, 14]], tbl_15[ids[:, 15]], tbl_16[ids[:, 16]], tbl_17[ids[:, 17]], tbl_18[ids[:, 18]], tbl_19[ids[:, 19]], tbl_20[ids[:, 20]], tbl_21[ids[:, 21]], tbl_22[ids[:, 22]], tbl_23[ids[:, 23]], tbl_24[ids[:, 24]], tbl_25[ids[:, 25]]], axis=1)
    z = _L0_rec_ref(r_bottom_output, e)
    z = z.reshape(z.shape[0], -1)
    h = jnp.concatenate([z, r_bottom_output], axis=1)
    h = jnp.maximum(h @ W_top1 + b_top1, 0.0)
    h = jnp.maximum(h @ W_top2 + b_top2, 0.0)
    y = h @ W_top3
    return y

_drawn_inputs = setup_inputs


def setup_inputs(seed=0):
    import zlib

    import numpy as np

    out = dict(_drawn_inputs(seed))
    spreads = {'b_top1': (0.0, 0.1), 'b_top2': (0.0, 0.1)}
    factors = {}
    for name, (base, spread) in spreads.items():
        noise = np.random.default_rng([zlib.crc32(name.encode()), seed]).standard_normal(out[name].shape)
        drawn = base * np.exp(spread * noise) if base else spread * noise
        out[name] = jnp.asarray(drawn.astype(out[name].dtype))
    for name, factor in factors.items():
        out[name] = (out[name] * factor).astype(out[name].dtype)
    return out
```

```python
import concourse.bass as bass
from concourse import mybir
from contextlib import ExitStack

P = 128
B = 512
T = B // P
D = 128
NF = 27
FP = 32
NJ = 4
Q = P // NJ
KOFF = (NF - 1) // 2
NE = NF + KOFF
KT = 3
FK = NF // KT
KR = FK * KOFF
H1, H2 = 512, 256
C1, C2 = H1 // P, H2 // P

ONEHOT = [1, 2, 3, 5, 7, 16, 18, 19]
GATHER = [f for f in range(26) if f not in ONEHOT]
NO = len(ONEHOT)
NG = len(GATHER)
SLOTS = [0] + [f + 1 for f in GATHER] + [f + 1 for f in ONEHOT]
OR = 8
OP = 125

TB = 4
BATCHES = [(s, min(s + TB, NG + 1)) for s in range(0, NG + 1, TB)]
NBT = len(BATCHES)
NBANK = 2
GH = 8
NH = Q // GH


def pair_rows():
    rows = []
    for s in range(NF):
        for k in range(1, KOFF + 1):
            a, b = sorted((SLOTS[s], SLOTS[(s + k) % NF]))
            rows.append(a * NF - a * (a + 1) // 2 + b - a - 1)
    return rows


def tower(nc, bottom, ids, ids_t, tbls, w1p, w1b, b1, w2, b2, w3, out):
    fp32, bf16, fp16, i32 = (mybir.dt.float32, mybir.dt.bfloat16, mybir.dt.float16, mybir.dt.int32)
    ALU = mybir.AluOpType
    ACT = mybir.ActivationFunctionType

    ctx = ExitStack()
    with ctx:
        def sb(name, shape, dt=fp32):
            return ctx.enter_context(nc.sbuf_tensor(name, shape, dt))

        def ps(name, shape):
            return ctx.enter_context(nc.psum_tensor(name, shape, fp32))

        def sem(name):
            return ctx.enter_context(nc.semaphore(name))

        z_dram = [nc.dram_tensor(f"z_dram{t}", (P, NE, Q), fp32, kind="Internal").ap() for t in range(T)]

        ident = sb("ident", [P, P])
        ids_sb = sb("ids_sb", [P, T, 26], i32)
        emb = sb("emb", [P, T, NG + 1, D])
        embT = sb("embT", [P, T, Q, NJ, FP])
        gram_sb = sb("gram_sb", [P, 2, NF, Q])
        zT = sb("zT", [P, 2, KT, P])
        w1p_sb = sb("w1p_sb", [P, KT, H1])
        w1b_sb = sb("w1b_sb", [P, H1])
        w2_sb = sb("w2_sb", [P, C1, H2])
        w3_sb = sb("w3_sb", [P, C2])
        b1_sb = sb("b1_sb", [P, C1])
        b2_sb = sb("b2_sb", [P, C2])
        h1_sb = sb("h1_sb", [P, C1, P])
        h2_sb = sb("h2_sb", [P, C2, P])
        y_sb = sb("y_sb", [1, B])
        row_i = sb("row_i", [P, OR], i32)
        row_f = sb("row_f", [P, OR])
        tbl_sb = sb("tbl_sb", [P, 2, OR, D])
        rest_sb = sb("rest_sb", [P, 2, OR, D])
        low_sb = sb("low_sb", [P, 2, OR, D], bf16)
        ids_bc = sb("ids_bc", [P, 2, B], i32)
        ids_h = sb("ids_h", [P, 2, B], fp16)
        hot = sb("hot", [P, 2, OR, B], bf16)

        feat_ps = [ps(f"feat_ps{i}", [P, TB * P]) for i in range(NBANK)]
        gram_ps = [ps(f"gram_ps{i}", [P, GH, P]) for i in range(2)]
        h1_ps = ps("h1_ps", [P, C1, P])
        h2_ps = ps("h2_ps", [P, C1, P])
        y_ps = h2_ps[0:1, C2, :]

        ids_in = sem("ids_in")
        bottom_in = sem("bottom_in")
        w1_in, w2_in, w3_in, bias_in = sem("w1_in"), sem("w2_in"), sem("w3_in"), sem("bias_in")
        tbl_in = [sem(f"tbl_in{i}") for i in range(2)]
        idbc_in = [sem(f"idbc_in{i}") for i in range(2)]
        gathered = [[sem(f"gathered{t}_{n}") for n in range(NBT)] for t in range(T)]
        const_set = sem("const_set")
        ident_zero = sem("ident_zero")
        row_ready = sem("row_ready")
        pad_zero = sem("pad_zero")
        idh_ready = sem("idh_ready")
        rest_ready = sem("rest_ready")
        split_ready = sem("split_ready")
        hot_ready = sem("hot_ready")
        feat_done = sem("feat_done")
        feat_out = {"act": sem("feat_out_act"), "dve": sem("feat_out_dve")}
        gram_done = sem("gram_done")
        gram_out = {"act": sem("gram_out_act"), "dve": sem("gram_out_dve")}
        z_written = [sem(f"z_written{t}") for t in range(T)]
        z_in = [sem(f"z_in{t}") for t in range(T)]
        l1_done, l2_done, l3_done = sem("l1_done"), sem("l2_done"), sem("l3_done")
        h1_out, h2_out = sem("h1_out"), sem("h2_out")
        y_out = sem("y_out")
        stored = sem("stored")
        block = ctx.enter_context(nc.Block())

        def taker(u):
            return "act" if u < NO or (u - NO) % 2 else "dve"

        def taken(u):
            e = taker(u)
            return feat_out[e], sum(taker(v) == e for v in range(u + 1))

        def wait_features(eng, last):
            for e in ("act", "dve"):
                n = sum(taker(v) == e for v in range(last + 1))
                if n:
                    eng.wait_ge(feat_out[e], n)

        def use(t, n):
            return NO + t * NBT + n

        def take_transposed(eng, copy, t, n):
            s0, s1 = BATCHES[n]
            u = use(t, n)
            eng.wait_ge(feat_done, u + 1)
            src = feat_ps[u % NBANK][:, 0:(s1 - s0) * P].rearrange("p (s j q) -> p j q s", s=s1 - s0, j=NJ)
            dst = embT[:, t, :, :, s0:s1].rearrange("p q j s -> p j q s")
            copy(dst, src).then_inc(feat_out[taker(u)], 1)

        def take_gram(eng, copy, t, h, quadrants, who):
            n = t * NH + h
            eng.wait_ge(gram_done, n + 1)
            if h == 0 and t >= 2:
                eng.wait_ge(z_written[t - 2], 32)
            for j in quadrants:
                last = copy(gram_sb[FP * j:FP * (j + 1), t % 2, :, h * GH:(h + 1) * GH],
                            gram_ps[n % 2][FP * j:FP * (j + 1), :, NF * j:NF * (j + 1)]
                            .rearrange("p q s -> p s q"))
            last.then_inc(gram_out[who], 1)

        def take_onehot(act, i):
            act.wait_ge(feat_done, i + 1)
            nc.scalar.copy(embT[:, :, :, :, NG + 1 + i].rearrange("p t q j -> p t j q"),
                           feat_ps[i % NBANK][:].rearrange("p (t j q) -> p t j q", t=T, j=NJ)).then_inc(feat_out["act"], 1)

        def dense_act(act, t):
            if t == 0:
                act.wait_ge(bias_in, 32)
            act.wait_ge(l2_done, t + 1)
            for m in range(C2):
                last = nc.scalar.activation(h2_sb[:, m, :], h2_ps[:, m, :], ACT.Relu, bias=b2_sb[:, m:m + 1])
            last.then_inc(h2_out, 1)
            act.wait_ge(l3_done, t + 1)
            nc.scalar.copy(y_sb[0:1, t * P:(t + 1) * P], y_ps).then_inc(y_out, 1)

        def dense_dve(dve, t):
            if t == 0:
                dve.wait_ge(bias_in, 32)
            dve.wait_ge(l1_done, t + 1)
            for c in range(C1):
                last = nc.vector.tensor_scalar(h1_sb[:, c, :], h1_ps[:, c, :], b1_sb[:, c:c + 1], 0.0,
                                               ALU.add, ALU.max)
            last.then_inc(h1_out, 1)

        @block.sync
        def _(sp):
            sp.dma_start(ids_sb[:], ids.rearrange("(t p) f -> p t f", p=P)).then_inc(ids_in, 16)

            def load_table(i):
                if i >= 2:
                    sp.wait_ge(feat_done, i - 1)
                sp.dma_start(ids_bc[:, i % 2, :], ids_t[ONEHOT[i]:ONEHOT[i] + 1, :].to_broadcast([P, B]))\
                  .then_inc(idbc_in[i % 2], 16)
                sp.dma_start(tbl_sb[0:OP, i % 2, :, :],
                             tbls[ONEHOT[i]].rearrange("(p r) d -> p r d", r=OR)).then_inc(tbl_in[i % 2], 16)

            for i in range(min(2, NO)):
                load_table(i)
            sp.dma_start(emb[:, :, 0, :], bottom.rearrange("(t p) d -> p t d", p=P)).then_inc(bottom_in, 16)
            sp.dma_start(w1p_sb[0:KR, :, :], w1p.rearrange("(k p) n -> p k n", p=KR)).then_inc(w1_in, 16)
            sp.dma_start(w1b_sb[:], w1b).then_inc(w1_in, 16)
            sp.dma_start(w2_sb[:], w2.rearrange("(k p) n -> p k n", p=P)).then_inc(w2_in, 16)
            with nc.allow_non_contiguous_dma(reason="a few hundred bias and W_top3 values"):
                sp.dma_start(b1_sb[:], b1.rearrange("(c p) -> p c", p=P)).then_inc(bias_in, 16)
                sp.dma_start(b2_sb[:], b2.rearrange("(c p) -> p c", p=P)).then_inc(bias_in, 16)
                sp.dma_start(w3_sb[:], w3.rearrange("(c p) o -> p (c o)", p=P)).then_inc(w3_in, 16)
            for i in range(2, NO):
                load_table(i)

            for t in range(T):
                for who in ("act", "dve"):
                    sp.wait_ge(gram_out[who], NH * (t + 1))
                sp.dma_start(z_dram[t][:, 0:NF, :], gram_sb[:, t % 2, :, :]).then_inc(z_written[t], 16)
                sp.dma_start(z_dram[t][:, NF:NE, :], gram_sb[:, t % 2, 0:KOFF, :]).then_inc(z_written[t], 16)
                sp.wait_ge(z_written[t], 32)
                if t >= 2:
                    sp.wait_ge(l1_done, t - 1)
                for k in range(KT):
                    for j in range(NJ):
                        src = bass.AP(z_dram[t].tensor,
                                      ((FP * j + FK * k) * NE + FK * k + 1) * Q,
                                      [[(NE + 1) * Q, FK], [Q, KOFF], [1, Q]])
                        sp.dma_start(zT[0:KR, t % 2, k, Q * j:Q * (j + 1)], src).then_inc(z_in[t], 16)
            sp.wait_ge(y_out, T)
            sp.dma_start(out.rearrange("b o -> o b"), y_sb[:]).then_inc(stored, 16)
            sp.wait_ge(stored, 16)

        @block.gpsimd
        def _(pool):
            pool.memset(ident[:], 0.0).then_inc(ident_zero, 1)
            pool.iota(row_i[:], pattern=[[1, OR]], base=0, channel_multiplier=OR).then_inc(const_set, 1)
            pool.wait_ge(ident_zero, 1)
            pool.affine_select(out=ident[:], in_=ident[:], compare_op=ALU.not_equal, fill=1.0, base=0,
                               pattern=[[-1, P]], channel_multiplier=1).then_inc(const_set, 1)
            pool.wait_ge(ids_in, 16)
            for t in range(T):
                for n, (s0, s1) in enumerate(BATCHES):
                    for s in range(max(s0, 1), s1):
                        f = GATHER[s - 1]
                        pool.indirect_dma_start(emb[:, t, s, :], None, tbls[f],
                                                bass.IndirectOffsetOnAxis(ids_sb[:, t, f:f + 1], 0))\
                            .then_inc(gathered[t][n], 16)

        @block.scalar
        def _(act):
            for i in range(NO):
                act.wait_ge(idbc_in[i % 2], 16 * (i // 2 + 1))
                if i >= 2:
                    act.wait_ge(hot_ready, i - 1)
                nc.scalar.copy(ids_h[0:OP, i % 2, :], ids_bc[0:OP, i % 2, :]).then_inc(idh_ready, 1)
                if i >= 1:
                    take_onehot(act, i - 1)
            take_onehot(act, NO - 1)
            for t in range(T):
                for n in range(NBT):
                    if taker(use(t, n)) == "act":
                        take_transposed(act, nc.scalar.copy, t, n)
                for h in range(NH):
                    take_gram(act, nc.scalar.copy, t, h, (2, 3), "act")
                if t >= 1:
                    dense_act(act, t - 1)
            dense_act(act, T - 1)

        @block.vector
        def _(dve):
            dve.wait_ge(const_set, 2)
            nc.vector.tensor_copy(row_f[:], row_i[:]).then_inc(row_ready, 1)
            nc.vector.memset(embT[:, :, :, :, NF:FP].rearrange("p t q j s -> p (t q j) s"), 0.0)\
                .then_inc(pad_zero, 1)
            for i in range(NO):
                b = i % 2
                upper = tbl_sb[0:OP, b].bitcast(bf16).rearrange("p r (d w) -> p r d w", w=2)[:, :, :, 1]
                middle = rest_sb[0:OP, b].bitcast(bf16).rearrange("p r (d w) -> p r d w", w=2)[:, :, :, 1]
                dve.wait_ge(tbl_in[b], 16 * (i // 2 + 1))
                if i >= 2:
                    dve.wait_ge(feat_done, i - 1)
                nc.vector.tensor_tensor(rest_sb[0:OP, b], tbl_sb[0:OP, b], upper, ALU.subtract)\
                    .then_inc(rest_ready, 1)
                dve.wait_ge(rest_ready, i + 1)
                nc.vector.tensor_tensor(low_sb[0:OP, b], rest_sb[0:OP, b], middle, ALU.subtract)\
                    .then_inc(split_ready, 1)
                dve.wait_ge(idh_ready, i + 1)
                if i == 0:
                    dve.wait_ge(row_ready, 1)
                for r in range(OR):
                    last = nc.vector.tensor_scalar(hot[0:OP, b, r, :], ids_h[0:OP, b, :], row_f[0:OP, r:r + 1],
                                                   None, ALU.is_equal)
                last.then_inc(hot_ready, 1)
            for t in range(T):
                for n in range(NBT):
                    if taker(use(t, n)) == "dve":
                        take_transposed(dve, nc.vector.tensor_copy, t, n)
                for h in range(NH):
                    take_gram(dve, nc.vector.tensor_copy, t, h, (0, 1), "dve")
                if t >= 1:
                    dense_dve(dve, t - 1)
            dense_dve(dve, T - 1)

        @block.tensor
        def _(pe):
            for i in range(NO):
                b = i % 2
                upper = tbl_sb[0:OP, b].bitcast(bf16).rearrange("p r (d w) -> p r d w", w=2)[:, :, :, 1]
                middle = rest_sb[0:OP, b].bitcast(bf16).rearrange("p r (d w) -> p r d w", w=2)[:, :, :, 1]
                parts = [upper, middle, low_sb[0:OP, b]]
                pe.wait_ge(split_ready, i + 1)
                pe.wait_ge(hot_ready, i + 1)
                if i >= NBANK:
                    pe.wait_ge(*taken(i - NBANK))
                for k, part in enumerate(parts):
                    for r in range(OR):
                        last = nc.tensor.matmul(feat_ps[i % NBANK][:], part[:, r, :], hot[0:OP, b, r, :],
                                                start=(k == 0 and r == 0), stop=(k == 2 and r == OR - 1))
                last.then_inc(feat_done, 1)

            def transposes(t):
                for n, (s0, s1) in enumerate(BATCHES):
                    u = use(t, n)
                    if n == 0 and t == 0:
                        pe.wait_ge(bottom_in, 16)
                        pe.wait_ge(const_set, 2)
                    pe.wait_ge(gathered[t][n], 16 * (s1 - max(s0, 1)))
                    if u >= NBANK:
                        pe.wait_ge(*taken(u - NBANK))
                    for s in range(s0, s1):
                        last = nc.tensor.transpose(feat_ps[u % NBANK][:, (s - s0) * P:(s - s0 + 1) * P],
                                                   emb[:, t, s, :], ident[:])
                    last.then_inc(feat_done, 1)

            def grams(t):
                wait_features(pe, use(t, NBT - 1))
                if t == 0:
                    pe.wait_ge(pad_zero, 1)
                for h in range(NH):
                    n = t * NH + h
                    if n >= 2:
                        for who in ("act", "dve"):
                            pe.wait_ge(gram_out[who], n - 1)
                    for g in range(GH):
                        q = h * GH + g
                        last = nc.tensor.matmul(
                            gram_ps[n % 2][:, g, 0:NJ * NF].rearrange("p (j s) -> p j s", j=NJ),
                            embT[:, t, q, :, :].rearrange("p j s -> p (j s)"), embT[:, t, q, :, 0:NF], start=True, stop=True)
                    last.then_inc(gram_done, 1)

            def dense(t):
                if t == 0:
                    pe.wait_ge(w1_in, 32)
                for c in range(C1):
                    nc.tensor.matmul(h1_ps[:, c, :].rearrange("p (j q) -> p j q", j=NJ), w1b_sb[:, c * P:(c + 1) * P],
                                     embT[:, t, :, :, 0].rearrange("p q j -> p j q"),
                                     start=(c == 0), stop=False, skip_group_check=True)
                pe.wait_ge(z_in[t], 16 * KT * NJ)
                for c in range(C1):
                    for k in range(KT):
                        last = nc.tensor.matmul(h1_ps[:, c, :], w1p_sb[0:KR, k, c * P:(c + 1) * P],
                                                zT[0:KR, t % 2, k, :], start=False, stop=(k == KT - 1),
                                                skip_group_check=True)
                last.then_inc(l1_done, 1)
                if t == 0:
                    pe.wait_ge(w2_in, 16)
                pe.wait_ge(h1_out, t + 1)
                if t >= 1:
                    pe.wait_ge(y_out, t)
                for m in range(C2):
                    for c in range(C1):
                        last = nc.tensor.matmul(h2_ps[:, m, :], w2_sb[:, c, m * P:(m + 1) * P], h1_sb[:, c, :],
                                                start=(c == 0), stop=(c == C1 - 1))
                last.then_inc(l2_done, 1)
                if t == 0:
                    pe.wait_ge(w3_in, 16)
                pe.wait_ge(h2_out, t + 1)
                for m in range(C2):
                    last = nc.tensor.matmul(y_ps, w3_sb[:, m:m + 1], h2_sb[:, m, :],
                                            start=(m == 0), stop=(m == C2 - 1))
                last.then_inc(l3_done, 1)

            for t in range(T):
                transposes(t)
                grams(t)
                if t >= 1:
                    dense(t - 1)
            dense(T - 1)


_TABLES = [f"tbl_{f}" for f in range(26)]


def kernel(**inputs):
    import numpy as _np
    import concourse.bacc as _bacc
    from concourse import mybir as _mybir
    from concourse.bass_utils import run_bass_kernel_spmd as _run

    nc = _bacc.Bacc("TRN2", target_bir_lowering=False, num_devices=1)
    pairs = KT * KR
    w1 = _np.asarray(inputs["W_top1"])
    ids = _np.asarray(inputs["ids"])
    laid = {
        "r_bottom_output": inputs["r_bottom_output"],
        "ids": ids,
        "ids_t": ids.T,
        **{name: inputs[name] for name in _TABLES},
        "w1_pairs": w1[pair_rows()],
        "w1_bottom": w1[pairs:],
        "b_top1": inputs["b_top1"], "W_top2": inputs["W_top2"], "b_top2": inputs["b_top2"],
        "W_top3": inputs["W_top3"],
    }
    arrays, aps = {}, {}
    for name, a in laid.items():
        a = _np.ascontiguousarray(a)
        arrays[f"in_{name}_dram"] = a
        aps[name] = nc.dram_tensor(f"in_{name}_dram", a.shape, _mybir.dt.from_np(a.dtype),
                                   kind="ExternalInput").ap()
    out = nc.dram_tensor("out_0_dram", (B, 1), _mybir.dt.float32, kind="ExternalOutput").ap()
    tower(nc, aps["r_bottom_output"], aps["ids"], aps["ids_t"], [aps[n] for n in _TABLES],
          aps["w1_pairs"], aps["w1_bottom"], aps["b_top1"], aps["W_top2"], aps["b_top2"],
          aps["W_top3"], out)
    r = _run(nc, [arrays], core_ids=[0])
    return r.results[0]["out_0_dram"]
```

```python
import concourse.bass as bass
from concourse import mybir
from contextlib import ExitStack

P = 128
B = 512
T = B // P
D = 128
NF = 27
FP = 32
NJ = 4
Q = P // NJ
HALF = NF // 2 + 1
NBLK = 3
H1, H2 = 512, 256
C1, C2 = H1 // P, H2 // P

ONEHOT = [1, 2, 3, 5, 7, 16]
GATHER = [f for f in range(26) if f not in ONEHOT]
NO = len(ONEHOT)
NG = len(GATHER)
NT = NG + 1
CUT = NBLK * 4
TURN_SLOTS = [*range(CUT), *range(HALF, HALF + NT - CUT)]
HOT_SLOTS = [CUT, CUT + 1, NF - 1, *range(HALF + NT - CUT, NF - 1)]
SLOTS = [None] * NF
for _n, _s in enumerate(TURN_SLOTS):
    SLOTS[_s] = 0 if _n == 0 else GATHER[_n - 1] + 1
for _n, _s in enumerate(HOT_SLOTS):
    SLOTS[_s] = ONEHOT[_n] + 1
ROWS = [*range(NF), CUT, CUT + 1, NF - 1, CUT + 1, NF - 1]
OR = 8
OP = 125

TB = 4
_CUTS = [0, TB, 2 * TB, CUT, CUT + TB, *range(CUT + 2 * TB, NT - 1, TB), NT - 1, NT]
BATCHES = list(zip(_CUTS[:-1], _CUTS[1:]))
NBT = len(BATCHES)
NBANK = 2
NTBL = 4
FIRST = 4
WARM = 10
GH = 8
PARTS = [[*range(0, Q + 1, GH)] for _ in range(T)]
PARTS[-1].insert(-1, Q - GH // 2)
PARTS = [list(zip(p[:-1], p[1:])) for p in PARTS]


def parts_before(t):
    return sum(len(p) for p in PARTS[:t])


def steps():
    hot = [("hot", i) for i in range(NO)]
    turn = [[("turn", t, n) for n in range(NBT)] for t in range(T)]
    out = hot[:2]
    for n, x in enumerate(hot[2:]):
        out += turn[0][n:n + 1] + [x]
    out += turn[0][NO - 2:]
    for t in range(T - 1):
        gram = [("gram", t, h) for h in range(len(PARTS[t]))]
        l1, l2, l3 = ([(layer, t)] for layer in ("l1", "l2", "l3"))
        nxt = turn[t + 1]
        if t == 0:
            out += nxt[:1] + gram[:1] + nxt[1:2] + gram[1:] + nxt[2:4] + l1 + nxt[4:5] + l2 + nxt[5:] + l3
        else:
            out += gram[:2] + nxt[:1] + gram[2:] + nxt[1:3] + l1 + nxt[3:4] + l2 + nxt[4:] + l3
    t = T - 1
    return out + [("gram", t, h) for h in range(len(PARTS[t]))] + [("l1", t), ("l2", t), ("l3", t)]


STEPS = steps()
TURNS = [x for x in STEPS if x[0] == "turn"]
TAKERS = ["act" if x[1] == 0 or x[2] % 2 == 0 else "dve" for x in TURNS]


def column(s, row):
    if row < NF:
        c = s if s < row < s + HALF else s + HALF
        return c if c != row else None
    if row < NF + 3:
        return s if ROWS[row] == NF - 1 else s + HALF
    if s == 0:
        return CUT
    return CUT + 1 if s == 1 and ROWS[row] == NF - 1 else None


def pair_place():
    places = []
    for a in range(4):
        for b in range(NBLK):
            for row in range(FP):
                c = column(4 * b + a, row)
                if c is not None:
                    i, j = sorted((SLOTS[ROWS[row]], SLOTS[c]))
                    places.append((FP * a + row, b, i * NF - i * (i + 1) // 2 + j - i - 1))
    return places


def tower(nc, bottom, ids, ids_t, tbls, w1p, w1b, b1, w2, b2, w3, out):
    fp32, bf16, fp16, i32 = (mybir.dt.float32, mybir.dt.bfloat16, mybir.dt.float16, mybir.dt.int32)
    ALU = mybir.AluOpType
    ACT = mybir.ActivationFunctionType

    ctx = ExitStack()
    with ctx:
        def sb(name, shape, dt=fp32):
            return ctx.enter_context(nc.sbuf_tensor(name, shape, dt))

        def ps(name, shape):
            return ctx.enter_context(nc.psum_tensor(name, shape, fp32))

        def sem(name):
            return ctx.enter_context(nc.semaphore(name))

        ident = sb("ident", [P, P])
        ids_sb = sb("ids_sb", [P, T, 26], i32)
        emb = sb("emb", [P, T, NG + 1, D])
        embT = sb("embT", [P, T, Q, NJ, FP])
        z_sb = sb("z_sb", [P, 2, 2, NBLK + 1, NJ, Q])
        place_i = sb("place_i", [P, NBLK + 1, NJ, GH], i32)
        far = sb("far", [P, NBLK, NJ, GH])
        row_no = sb("row_no", [P, NJ, GH])
        main_row = sb("main_row", [P, 1])
        other = sb("other", [P, NBLK, NJ, GH], i32)
        corner = sb("corner", [P, NJ, GH], i32)
        w1p_sb = sb("w1p_sb", [P, NBLK, H1])
        w1b_sb = sb("w1b_sb", [P, H1])
        w2_sb = sb("w2_sb", [P, C1, H2])
        w3_sb = sb("w3_sb", [P, C2])
        b1_sb = sb("b1_sb", [P, C1])
        b2_sb = sb("b2_sb", [P, C2])
        h1_sb = sb("h1_sb", [P, C1, P])
        h2_sb = sb("h2_sb", [P, C2, P])
        y_sb = sb("y_sb", [1, B])
        warm_sb = sb("warm_sb", [P, B], bf16)
        row_i = sb("row_i", [P, OR], i32)
        row_f = sb("row_f", [P, OR])
        tbl_sb = sb("tbl_sb", [P, NTBL, OR, D])
        rest_sb = sb("rest_sb", [P, 2, OR, D])
        low_sb = sb("low_sb", [P, 2, OR, D], bf16)
        ids_bc = sb("ids_bc", [P, NTBL, B], i32)
        ids_h = sb("ids_h", [P, 2, B], fp16)
        hot = sb("hot", [P, 2, OR, B], bf16)

        turn_ps = [ps(f"turn_ps{i}", [P, TB * P]) for i in range(NBANK)]
        gram_ps = [ps(f"gram_ps{i}", [P, GH, P]) for i in range(2)]
        low_ps = ps("low_ps", [P, 4, P])
        high_ps = ps("high_ps", [P, 4, P])
        h1_ps = [low_ps[:, 0, :], low_ps[:, 1, :], high_ps[:, 0, :], high_ps[:, 1, :]]
        h2_ps = [low_ps[:, 2, :], high_ps[:, 2, :]]
        y_ps = high_ps[0:1, 3, :]

        ids_in = sem("ids_in")
        bottom_in = sem("bottom_in")
        w1_in, w2_in, w3_in, bias_in = sem("w1_in"), sem("w2_in"), sem("w3_in"), sem("bias_in")
        tbl_in = [sem(f"tbl_in{i}") for i in range(NTBL)]
        first_in = sem("first_in")
        idbc_in = [sem(f"idbc_in{i}") for i in range(NTBL)]
        gathered = [[sem(f"gathered{t}_{n}") for n in range(NBT)] for t in range(T)]
        const_set = sem("const_set")
        ident_zero = sem("ident_zero")
        place_set = sem("place_set")
        row_ready = sem("row_ready")
        idh_ready = sem("idh_ready")
        rest_ready = sem("rest_ready")
        low_ready = sem("low_ready")
        hot_ready = sem("hot_ready")
        warm_ready = sem("warm_ready")
        place_ready = sem("place_ready")
        other_ready = sem("other_ready")
        merged = sem("merged")
        z_ready = sem("z_ready")
        turn_done = sem("turn_done")
        hot_done = sem("hot_done")
        hot_out = sem("hot_out")
        turn_out = {"act": sem("turn_out_act"), "dve": sem("turn_out_dve")}
        gram_done = sem("gram_done")
        gram_out = {"act": sem("gram_out_act"), "dve": sem("gram_out_dve")}
        l1_done, l2_done, l3_done = sem("l1_done"), sem("l2_done"), sem("l3_done")
        h1_act, h1_dve, h2_act, h2_dve = sem("h1_act"), sem("h1_dve"), sem("h2_act"), sem("h2_dve")
        y_out = sem("y_out")
        stored = sem("stored")
        block = ctx.enter_context(nc.Block())

        def wait_turned(eng, u):
            e = TAKERS[u]
            eng.wait_ge(turn_out[e], sum(TAKERS[v] == e for v in range(u + 1)))

        def wait_features(eng, t):
            last = TURNS.index(("turn", t, NBT - 1))
            for e in ("act", "dve"):
                n = sum(TAKERS[v] == e for v in range(last + 1))
                if n:
                    eng.wait_ge(turn_out[e], n)
            if t == 0:
                eng.wait_ge(hot_out, NO)

        def take_turn(eng, copy, x):
            u = TURNS.index(x)
            s0, s1 = BATCHES[x[2]]
            eng.wait_ge(turn_done, u + 1)
            src = turn_ps[u % NBANK][:, 0:(s1 - s0) * P].rearrange("p (s j q) -> p j q s", s=s1 - s0, j=NJ)
            first = TURN_SLOTS[s0]
            dst = embT[:, x[1], :, :, first:first + s1 - s0].rearrange("p q j s -> p j q s")
            copy(dst, src).then_inc(turn_out[TAKERS[u]], 1)

        def hot_bank(i):
            return gram_ps[i % 2][:, 0:TB, :].rearrange("p g c -> p (g c)")

        def take_gram(eng, copy, t, h, quadrants, who):
            n = parts_before(t) + h
            q0, q1 = PARTS[t][h]
            eng.wait_ge(gram_done, n + 1)
            if h == 0 and t >= 2:
                eng.wait_ge(l1_done, 2 * (t - 1))
            for j in quadrants:
                own = gram_ps[q0 // GH % 2][FP * j:FP * (j + 1), q0 % GH:q0 % GH + q1 - q0, FP * j:FP * (j + 1)]\
                    .rearrange("p q (w b a) -> p w b q a", w=2, a=4)
                for a in range(4):
                    nb = NBLK + (a < 2)
                    last = copy(z_sb[FP * a:FP * (a + 1), t % 2, :, 0:nb, j, q0:q1],
                                own[:, :, 0:nb, :, a])
            last.then_inc(gram_out[who], 1)

        def merge(dve, t, m):
            parts = parts_before(t) + sum(q1 <= (m + 1) * GH for _, q1 in PARTS[t])
            for e in ("act", "dve"):
                dve.wait_ge(gram_out[e], parts)
            if t == 0 and m == 0:
                dve.wait_ge(other_ready, 1)
            part = z_sb[:, t % 2, :, :, :, m * GH:(m + 1) * GH]
            nc.vector.copy_predicated(part[:, 0, 0], other[:, 0], part[:, 1, 0]).then_inc(merged, 1)
            nc.vector.copy_predicated(part[:, 0, 1:NBLK], other[:, 1:NBLK], part[:, 1, 1:NBLK])
            dve.wait_ge(merged, t * (Q // GH) + m + 1)
            nc.vector.copy_predicated(part[0:2 * FP, 0, 0], corner[0:2 * FP], part[0:2 * FP, 0, NBLK])\
                .then_inc(z_ready, 1)

        def place_masks(dve):
            dve.wait_ge(place_set, 1)
            for a in range(4):
                quad = slice(FP * a, FP * (a + 1))
                nc.vector.tensor_scalar(far[quad], place_i[quad, 0:NBLK], float(-FP * a - a - HALF // 2), None,
                                        ALU.add).then_inc(place_ready, 1)
                nc.vector.tensor_scalar(row_no[quad], place_i[quad, 0], float(-FP * a), None, ALU.add)\
                    .then_inc(place_ready, 1)
            dve.wait_ge(place_ready, 8)
            nc.vector.tensor_tensor(far[:], far[:], far[:], ALU.mult).then_inc(place_ready, 1)
            nc.vector.tensor_scalar(main_row[:], row_no[:, 0, 0:1], NF + 1.5, None, ALU.is_lt).then_inc(place_ready, 1)
            nc.vector.tensor_scalar(corner[:], row_no[:], NF + 2.5, None, ALU.is_gt)
            dve.wait_ge(place_ready, 10)
            nc.vector.tensor_scalar(other[:], far[:], float((HALF // 2 - 1) ** 2) + 0.5, main_row[:, 0:1],
                                    ALU.is_gt, ALU.mult).then_inc(other_ready, 1)

        def relu(eng, who, out, src, bias):
            if who == "act":
                return nc.scalar.activation(out, src, ACT.Relu, bias=bias)
            return nc.vector.tensor_scalar(out, src, bias, 0.0, ALU.add, ALU.max)

        def layer1_out(eng, who, t):
            first, done = (0, h1_act) if who == "act" else (2, h1_dve)
            if t == 0:
                eng.wait_ge(bias_in, 32)
            eng.wait_ge(l1_done, 2 * t + 1 + (who == "dve"))
            for c in (first, first + 1):
                last = relu(eng, who, h1_sb[:, c, :], h1_ps[c], b1_sb[:, c:c + 1])
            last.then_inc(done, 1)

        def layer2_out(eng, who, t):
            m, done = (0, h2_act) if who == "act" else (1, h2_dve)
            eng.wait_ge(l2_done, 2 * t + 1 + m)
            relu(eng, who, h2_sb[:, m, :], h2_ps[m], b2_sb[:, m:m + 1]).then_inc(done, 1)

        @block.sync
        def _(sp):
            def load_table(i):
                if i >= NTBL:
                    sp.wait_ge(hot_done, i - NTBL + 1)
                sp.dma_start(ids_bc[:, i % NTBL, :], ids_t[ONEHOT[i]:ONEHOT[i] + 1, :].to_broadcast([P, B]))\
                  .then_inc(idbc_in[i % NTBL], 16)
                table = tbls[ONEHOT[i]].rearrange("(p r) d -> p r d", r=OR)
                first = FIRST if i == 0 else 0
                if i == 0:
                    sp.dma_start(tbl_sb[0:OP, 0, 0:first, :], table[:, 0:first, :]).then_inc(first_in, 16)
                sp.dma_start(tbl_sb[0:OP, i % NTBL, first:, :], table[:, first:, :]).then_inc(tbl_in[i % NTBL], 16)

            sp.dma_start(ids_sb[:], ids.rearrange("(p t) f -> p t f", p=P)).then_inc(ids_in, 16)
            load_table(0)
            load_table(1)
            sp.dma_start(emb[:, :, 0, :], bottom.rearrange("(p t) d -> p t d", p=P)).then_inc(bottom_in, 16)
            load_table(2)
            load_table(3)
            sp.dma_start(w1p_sb[:], w1p).then_inc(w1_in, 16)
            sp.dma_start(w1b_sb[:], w1b).then_inc(w1_in, 16)
            sp.dma_start(w2_sb[:], w2.rearrange("(k p) n -> p k n", p=P)).then_inc(w2_in, 16)
            with nc.allow_non_contiguous_dma(reason="a few hundred bias and W_top3 values"):
                sp.dma_start(b1_sb[:], b1.rearrange("(c p) -> p c", p=P)).then_inc(bias_in, 16)
                sp.dma_start(b2_sb[:], b2.rearrange("(c p) -> p c", p=P)).then_inc(bias_in, 16)
                sp.dma_start(w3_sb[:], w3.rearrange("(c p) o -> p (c o)", p=P)).then_inc(w3_in, 16)
            for i in range(NTBL, NO):
                load_table(i)

            sp.wait_ge(y_out, T)
            sp.dma_start(out.rearrange("b o -> o b"), y_sb[:]).then_inc(stored, 16)
            sp.wait_ge(stored, 16)

        @block.gpsimd
        def _(pool):
            pool.memset(ident[:], 0.0).then_inc(ident_zero, 1)
            pool.iota(row_i[:], pattern=[[1, OR]], base=0, channel_multiplier=OR).then_inc(const_set, 1)
            pool.iota(place_i[:], pattern=[[-4, NBLK + 1], [0, NJ], [0, GH]], base=0,
                      channel_multiplier=1).then_inc(place_set, 1)
            pool.wait_ge(ident_zero, 1)
            pool.affine_select(out=ident[:], in_=ident[:], compare_op=ALU.not_equal, fill=1.0, base=0,
                               pattern=[[-1, P]], channel_multiplier=1).then_inc(const_set, 1)
            pool.wait_ge(ids_in, 16)
            for t in range(T):
                for n, (s0, s1) in enumerate(BATCHES):
                    for s in range(max(s0, 1), s1):
                        f = GATHER[s - 1]
                        pool.indirect_dma_start(emb[:, t, s, :], None, tbls[f],
                                                bass.IndirectOffsetOnAxis(ids_sb[:, t, f:f + 1], 0))\
                            .then_inc(gathered[t][n], 16)

        @block.scalar
        def _(act):
            def cast_ids(i):
                act.wait_ge(idbc_in[i % NTBL], 16 * (i // NTBL + 1))
                if i >= 2:
                    act.wait_ge(hot_ready, OR * (i - 1))
                nc.scalar.copy(ids_h[0:OP, i % 2, :], ids_bc[0:OP, i % NTBL, :]).then_inc(idh_ready, 1)

            cast_ids(0)
            for x in STEPS:
                if x[0] == "hot" and x[1] + 1 < NO:
                    cast_ids(x[1] + 1)
                if x[0] == "hot":
                    i = x[1]
                    act.wait_ge(hot_done, i + 1)
                    for row in [n for n in range(FP) if ROWS[n] == HOT_SLOTS[i]]:
                        last = nc.scalar.copy(embT[:, :, :, :, row].rearrange("p t q j -> p t j q"),
                                              hot_bank(i).rearrange("p (j q t) -> p t j q", t=T, j=NJ))
                    last.then_inc(hot_out, 1)
                elif x[0] == "turn" and TAKERS[TURNS.index(x)] == "act":
                    take_turn(act, nc.scalar.copy, x)
                elif x[0] == "gram":
                    take_gram(act, nc.scalar.copy, x[1], x[2], (2, 3), "act")
                elif x[0] == "l1":
                    layer1_out(act, "act", x[1])
                elif x[0] == "l2":
                    layer2_out(act, "act", x[1])
                elif x[0] == "l3":
                    t = x[1]
                    act.wait_ge(l3_done, t + 1)
                    nc.scalar.copy(y_sb[:].rearrange("o (p t) -> o p t", t=T)[:, :, t], y_ps).then_inc(y_out, 1)

        @block.vector
        def _(dve):
            nc.vector.memset(warm_sb[:], 0.0).then_inc(warm_ready, 1)
            dve.wait_ge(const_set, 2)
            nc.vector.tensor_copy(row_f[:], row_i[:]).then_inc(row_ready, 1)
            dve.wait_ge(row_ready, 1)
            for i in range(NO):
                b, a = i % 2, i % NTBL
                upper = tbl_sb[0:OP, a].bitcast(bf16).rearrange("p r (d w) -> p r d w", w=2)[:, :, :, 1]
                middle = rest_sb[0:OP, b].bitcast(bf16).rearrange("p r (d w) -> p r d w", w=2)[:, :, :, 1]
                dve.wait_ge(idh_ready, i + 1)
                if i >= 2:
                    dve.wait_ge(hot_done, i - 1)
                for r in range(OR):
                    nc.vector.tensor_scalar(hot[0:OP, b, r, :], ids_h[0:OP, b, :], row_f[0:OP, r:r + 1],
                                            None, ALU.is_equal).then_inc(hot_ready, 1)
                if i == 0:
                    dve.wait_ge(first_in, 16)
                dve.wait_ge(tbl_in[a], 16 * (i // NTBL + 1))
                nc.vector.tensor_tensor(rest_sb[0:OP, b], tbl_sb[0:OP, a], upper, ALU.subtract)\
                    .then_inc(rest_ready, 1)
                dve.wait_ge(rest_ready, i + 1)
                nc.vector.tensor_tensor(low_sb[0:OP, b], rest_sb[0:OP, b], middle, ALU.subtract)\
                    .then_inc(low_ready, 1)
                if i == 1:
                    place_masks(dve)
            for x in STEPS:
                if x[0] == "turn" and TAKERS[TURNS.index(x)] == "dve":
                    take_turn(dve, nc.vector.tensor_copy, x)
                elif x[0] == "gram":
                    t = x[1]
                    take_gram(dve, nc.vector.tensor_copy, t, x[2], (0, 1), "dve")
                    if x[2] >= 1 and PARTS[t][x[2]][0] % GH == 0:
                        merge(dve, t, PARTS[t][x[2]][0] // GH - 1)
                    if x[2] == len(PARTS[t]) - 1:
                        merge(dve, t, Q // GH - 1)
                elif x[0] == "l1":
                    layer1_out(dve, "dve", x[1])
                elif x[0] == "l2":
                    layer2_out(dve, "dve", x[1])

        @block.tensor
        def _(pe):
            pe.wait_ge(warm_ready, 1)
            for _ in range(WARM):
                nc.tensor.matmul(turn_ps[0][:], warm_sb[:, 0:P], warm_sb[:], start=True, stop=True)

            def hot_table(i):
                b, a, bank = i % 2, i % NTBL, hot_bank(i)
                upper = tbl_sb[0:OP, a].bitcast(bf16).rearrange("p r (d w) -> p r d w", w=2)[:, :, :, 1]
                middle = rest_sb[0:OP, b].bitcast(bf16).rearrange("p r (d w) -> p r d w", w=2)[:, :, :, 1]
                if i == 0:
                    pe.wait_ge(first_in, 16)
                if i >= 2:
                    pe.wait_ge(hot_out, i - 1)
                for r in range(OR):
                    if r == (FIRST if i == 0 else 0):
                        pe.wait_ge(tbl_in[a], 16 * (i // NTBL + 1))
                    pe.wait_ge(hot_ready, OR * i + r + 1)
                    nc.tensor.matmul(bank, upper[:, r, :], hot[0:OP, b, r, :],
                                     start=(r == 0), stop=False)
                pe.wait_ge(rest_ready, i + 1)
                for r in range(OR):
                    nc.tensor.matmul(bank, middle[:, r, :], hot[0:OP, b, r, :],
                                     start=False, stop=False)
                pe.wait_ge(low_ready, i + 1)
                for r in range(OR):
                    last = nc.tensor.matmul(bank, low_sb[0:OP, b, r, :], hot[0:OP, b, r, :],
                                            start=False, stop=(r == OR - 1))
                last.then_inc(hot_done, 1)

            def transposes(t, n):
                s0, s1 = BATCHES[n]
                u = TURNS.index(("turn", t, n))
                if n == 0 and t == 0:
                    pe.wait_ge(bottom_in, 16)
                    pe.wait_ge(const_set, 2)
                pe.wait_ge(gathered[t][n], 16 * (s1 - max(s0, 1)))
                if u >= NBANK:
                    wait_turned(pe, u - NBANK)
                for s in range(s0, s1):
                    last = nc.tensor.transpose(turn_ps[u % NBANK][:, (s - s0) * P:(s - s0 + 1) * P],
                                               emb[:, t, s, :], ident[:])
                last.then_inc(turn_done, 1)

            def gram(t, h):
                if h == 0:
                    wait_features(pe, t)
                n = parts_before(t) + h
                slot_used = n - 1 if PARTS[t][h][0] % GH == 0 else n - 2
                if slot_used > 0:
                    for who in ("act", "dve"):
                        pe.wait_ge(gram_out[who], slot_used)
                q0, q1 = PARTS[t][h]
                for q in range(q0, q1):
                    own = embT[:, t, q, :, :]
                    moving = bass.AP(own.tensor, own.offset, [own.ap[0], [FP, NJ], [HALF, 2], [1, 16]])
                    last = nc.tensor.matmul(
                        gram_ps[q // GH % 2][:, q % GH, :].rearrange("p (j w s) -> p j w s", j=NJ, w=2),
                        own.rearrange("p j s -> p (j s)"), moving, start=True, stop=True)
                last.then_inc(gram_done, 1)

            def layer1(t):
                if t == 0:
                    pe.wait_ge(w1_in, 32)
                else:
                    pe.wait_ge(y_out, t)
                for c in range(C1):
                    nc.tensor.matmul(h1_ps[c].rearrange("p (j q) -> p j q", j=NJ),
                                     w1b_sb[:, c * P:(c + 1) * P],
                                     embT[:, t, :, :, 0].rearrange("p q j -> p j q"),
                                     start=(c % 2 == 0), stop=False, skip_group_check=True)
                pe.wait_ge(z_ready, Q // GH * (t + 1))
                for c in range(C1):
                    for b in range(NBLK):
                        last = nc.tensor.matmul(h1_ps[c], w1p_sb[:, b, c * P:(c + 1) * P],
                                                z_sb[:, t % 2, 0, b, :, :].rearrange("p j q -> p (j q)"),
                                                start=False, stop=(b == NBLK - 1), skip_group_check=True)
                    if c % 2:
                        last.then_inc(l1_done, 1)

            def layer2(t):
                if t == 0:
                    pe.wait_ge(w2_in, 16)
                pe.wait_ge(h1_act, t + 1)
                for m in range(C2):
                    for c in range(C1):
                        if m == 0 and c == 2:
                            pe.wait_ge(h1_dve, t + 1)
                        last = nc.tensor.matmul(h2_ps[m], w2_sb[:, c, m * P:(m + 1) * P], h1_sb[:, c, :],
                                                start=(c == 0), stop=(c == C1 - 1))
                    last.then_inc(l2_done, 1)

            def layer3(t):
                if t == 0:
                    pe.wait_ge(w3_in, 16)
                pe.wait_ge(h2_act, t + 1)
                pe.wait_ge(h2_dve, t + 1)
                for m in range(C2):
                    last = nc.tensor.matmul(y_ps, w3_sb[:, m:m + 1], h2_sb[:, m, :],
                                            start=(m == 0), stop=(m == C2 - 1))
                last.then_inc(l3_done, 1)

            for x in STEPS:
                if x[0] == "hot":
                    hot_table(x[1])
                elif x[0] == "turn":
                    transposes(x[1], x[2])
                elif x[0] == "gram":
                    gram(x[1], x[2])
                elif x[0] == "l1":
                    layer1(x[1])
                elif x[0] == "l2":
                    layer2(x[1])
                else:
                    layer3(x[1])


_TABLES = [f"tbl_{f}" for f in range(26)]


def kernel(**inputs):
    import numpy as _np
    import concourse.bacc as _bacc
    from concourse import mybir as _mybir
    from concourse.bass_utils import run_bass_kernel_spmd as _run

    nc = _bacc.Bacc("TRN2", target_bir_lowering=False, num_devices=1)
    pairs = NF * (NF - 1) // 2
    w1 = _np.asarray(inputs["W_top1"])
    ids = _np.asarray(inputs["ids"])
    w1_pairs = _np.zeros((P, NBLK, H1), w1.dtype)
    for part, block, row in pair_place():
        w1_pairs[part, block] = w1[row]
    laid = {
        "r_bottom_output": inputs["r_bottom_output"],
        "ids": ids,
        "ids_t": ids.T,
        **{name: inputs[name] for name in _TABLES},
        "w1_pairs": w1_pairs,
        "w1_bottom": w1[pairs:],
        "b_top1": inputs["b_top1"], "W_top2": inputs["W_top2"], "b_top2": inputs["b_top2"],
        "W_top3": inputs["W_top3"],
    }
    arrays, aps = {}, {}
    for name, a in laid.items():
        a = _np.ascontiguousarray(a)
        arrays[f"in_{name}_dram"] = a
        aps[name] = nc.dram_tensor(f"in_{name}_dram", a.shape, _mybir.dt.from_np(a.dtype),
                                   kind="ExternalInput").ap()
    out = nc.dram_tensor("out_0_dram", (B, 1), _mybir.dt.float32, kind="ExternalOutput").ap()
    tower(nc, aps["r_bottom_output"], aps["ids"], aps["ids_t"], [aps[n] for n in _TABLES],
          aps["w1_pairs"], aps["w1_bottom"], aps["b_top1"], aps["W_top2"], aps["b_top2"],
          aps["W_top3"], out)
    r = _run(nc, [arrays], core_ids=[0])
    return r.results[0]["out_0_dram"]
```

```python
import concourse.bass as bass
from concourse import mybir
from contextlib import ExitStack

P = 128
B = 512
T = B // P
D = 128
NF = 27
FP = 32
NJ = 4
Q = P // NJ
HALF = NF // 2 + 1
NBLK = 3
H1, H2 = 512, 256
C1, C2 = H1 // P, H2 // P

ONEHOT = [1, 2, 3, 5, 7, 16, 18]
LATE, LATE_T = 19, 2
GATHER = [f for f in range(26) if f not in ONEHOT + [LATE]] + [LATE]
NG = len(GATHER)
NT = NG + 1
CUT = NBLK * 4
TURN_SLOTS = [*range(CUT), *range(HALF, HALF + NT - CUT)]
HOT_SLOTS = [CUT, CUT + 1, NF - 1, *range(HALF + NT - CUT, NF - 1)]
SLOTS = [None] * NF
for _n, _s in enumerate(TURN_SLOTS):
    SLOTS[_s] = 0 if _n == 0 else GATHER[_n - 1] + 1
for _n, _s in enumerate(HOT_SLOTS):
    SLOTS[_s] = ONEHOT[_n] + 1
LOOKUPS = [(LATE, TURN_SLOTS[-1], LATE_T), *((f, s, 0) for f, s in zip(ONEHOT, HOT_SLOTS))]
NO = len(LOOKUPS)
ROWS = [*range(NF), CUT, CUT + 1, NF - 1, CUT + 1, NF - 1]
OR = 8
OP = 1000 // OR

TB = 4
BATCHES = []
for _t in range(T):
    _n = NT if _t < LATE_T else NT - 1
    _cuts = [0, TB, 2 * TB, CUT, *range(CUT + TB, _n - 1, TB), _n - 1, _n]
    BATCHES.append(list(zip(_cuts[:-1], _cuts[1:])))
NBT = len(BATCHES[0])
NBANK = 2
NTBL = 3
FIRST = OR // 2
WARM = 10
GH = 8
NPART = Q // GH
MERGES = [[[], [(0, 1)], [(1, 2)], [(2, 3), (3, 4)]]] * (T - 1) + [[[], [(0, 2)], [(2, 3)], [(3, 4)]]]
MG = 2


def steps():
    hot = [("hot", i) for i in range(NO)]
    turn = [[("turn", t, n) for n in range(NBT)] for t in range(T)]
    out = hot[:2]
    for n, x in enumerate(hot[2:]):
        out += turn[0][n:n + 1] + [x]
    out += turn[0][NO - 2:]
    for t in range(T - 1):
        gram = [("gram", t, h) for h in range(NPART)]
        l1, l2, l3 = ([(layer, t)] for layer in ("l1", "l2", "l3"))
        nxt = turn[t + 1]
        if t == 0:
            out += nxt[:1] + gram[:1] + nxt[1:2] + gram[1:] + nxt[2:4] + l1 + nxt[4:5] + l2 + nxt[5:] + l3
        else:
            out += gram[:2] + nxt[:1] + gram[2:] + nxt[1:3] + l1 + nxt[3:4] + l2 + nxt[4:] + l3
    t = T - 1
    return out + [("gram", t, h) for h in range(NPART)] + [("l1", t), ("l2", t), ("l3", t)]


STEPS = steps()
TURNS = [x for x in STEPS if x[0] == "turn"]
TAKERS = ["act" if x[1] == 0 or x[2] % 2 == 0 else "dve" for x in TURNS]


def column(s, row):
    if row < NF:
        c = s if s < row < s + HALF else s + HALF
        return c if c != row else None
    if row < NF + 3:
        return s if ROWS[row] == NF - 1 else s + HALF
    if s == 0:
        return CUT
    return CUT + 1 if s == 1 and ROWS[row] == NF - 1 else None


def pair_place():
    places = []
    for a in range(4):
        for b in range(NBLK):
            for row in range(FP):
                c = column(4 * b + a, row)
                if c is not None:
                    i, j = sorted((SLOTS[ROWS[row]], SLOTS[c]))
                    places.append((FP * a + row, b, i * NF - i * (i + 1) // 2 + j - i - 1))
    return places


def tower(nc, bottom, ids, ids_t, tbls, w1p, w1b, b1, w2, b2, w3, out):
    fp32, fp32r, bf16, i32 = (mybir.dt.float32, mybir.dt.float32r, mybir.dt.bfloat16, mybir.dt.int32)
    ALU = mybir.AluOpType
    ACT = mybir.ActivationFunctionType

    ctx = ExitStack()
    with ctx:
        def sb(name, shape, dt=fp32):
            return ctx.enter_context(nc.sbuf_tensor(name, shape, dt))

        def ps(name, shape):
            return ctx.enter_context(nc.psum_tensor(name, shape, fp32))

        def sem(name):
            return ctx.enter_context(nc.semaphore(name))

        ident = sb("ident", [P, P])
        ids_sb = sb("ids_sb", [P, T, 26], i32)
        emb = sb("emb", [P, T, NT, D])
        embT = sb("embT", [P, T, Q, NJ, FP])
        z_sb = sb("z_sb", [P, 2, 2, NBLK + 1, NJ, Q])
        place_i = sb("place_i", [P, NBLK + 1, NJ, MG * GH], i32)
        far = sb("far", [P, NBLK, NJ, MG * GH])
        row_no = sb("row_no", [P, NJ, MG * GH])
        main_row = sb("main_row", [P, 1])
        other = sb("other", [P, NBLK, NJ, MG * GH], i32)
        corner = sb("corner", [P, NJ, MG * GH], i32)
        w1p_sb = sb("w1p_sb", [P, NBLK, H1])
        w1b_sb = sb("w1b_sb", [P, H1])
        w2_sb = sb("w2_sb", [P, C1, H2])
        w3_sb = sb("w3_sb", [P, C2])
        b1_sb = sb("b1_sb", [P, C1])
        b2_sb = sb("b2_sb", [P, C2])
        h1_sb = sb("h1_sb", [P, C1, P])
        h2_sb = sb("h2_sb", [P, C2, P])
        y_sb = sb("y_sb", [1, B])
        warm_sb = sb("warm_sb", [P, B], bf16)
        row_i = sb("row_i", [P, OR], i32)
        row_f = sb("row_f", [P, OR])
        tbl_sb = sb("tbl_sb", [P, NTBL, OR, D])
        upper_sb = sb("upper_sb", [P, 2, OR, D], fp32r)
        lower_sb = sb("lower_sb", [P, 2, OR, D], fp32r)
        ids_bc = sb("ids_bc", [P, NTBL, 2, B], i32)
        hot = sb("hot", [P, 2, OR, B], fp32r)

        turn_ps = [ps(f"turn_ps{i}", [P, TB * P]) for i in range(NBANK)]
        gram_ps = [ps(f"gram_ps{i}", [P, GH, P]) for i in range(2)]
        low_ps = ps("low_ps", [P, 4, P])
        high_ps = ps("high_ps", [P, 4, P])

        h2_ps = [low_ps[:, 2, :], high_ps[:, 2, :]]
        y_ps = low_ps[0:1, 3, :]

        def h1_ps(t, c):
            if t < T - 1:
                return (low_ps, high_ps)[c // 2][:, c % 2, :]
            return [low_ps[:, 0, :], high_ps[:, 0, :], turn_ps[0][:, 0:P], turn_ps[1][:, 0:P]][c]

        def h1_taker(t, c):
            return ("act", "dve")[c % 2 if t == T - 1 else c // 2]

        def h1_shared(t, c):
            return c + 1 if t == T - 1 else c // 2 * 2 + 2

        ids_in = sem("ids_in")
        bottom_in = sem("bottom_in")
        w1_in, w2_in, w3_in, bias_in = sem("w1_in"), sem("w2_in"), sem("w3_in"), sem("bias_in")
        tbl_in = [sem(f"tbl_in{i}") for i in range(NTBL)]
        first_in = sem("first_in")
        idbc_in = [sem(f"idbc_in{i}") for i in range(NTBL)]
        gathered = [[sem(f"gathered{t}_{n}") for n in range(NBT)] for t in range(T)]
        const_set = sem("const_set")
        ident_zero = sem("ident_zero")
        place_set = sem("place_set")
        row_ready = sem("row_ready")
        less_ready = sem("less_ready")
        upper_ready = sem("upper_ready")
        lower_ready = sem("lower_ready")
        hot_ready = sem("hot_ready")
        warm_ready = sem("warm_ready")
        place_ready = sem("place_ready")
        other_ready = sem("other_ready")
        merged = sem("merged")
        z_rest_ready = sem("z_rest_ready")
        z0_ready = sem("z0_ready")
        turn_done = sem("turn_done")
        hot_done = sem("hot_done")
        hot_out = sem("hot_out")
        turn_out = {"act": sem("turn_out_act"), "dve": sem("turn_out_dve")}
        gram_done = sem("gram_done")
        gram_out = {"act": sem("gram_out_act"), "dve": sem("gram_out_dve")}
        l1_done, l2_done, l3_done = sem("l1_done"), sem("l2_done"), sem("l3_done")
        h1_ready = {"act": sem("h1_act"), "dve": sem("h1_dve")}
        h2_act, h2_dve = sem("h2_act"), sem("h2_dve")
        y_out = sem("y_out")
        stored = sem("stored")
        block = ctx.enter_context(nc.Block())

        def wait_turned(eng, u):
            e = TAKERS[u]
            eng.wait_ge(turn_out[e], sum(TAKERS[v] == e for v in range(u + 1)))

        def wait_features(eng, t):
            last = TURNS.index(("turn", t, NBT - 1))
            for e in ("act", "dve"):
                n = sum(TAKERS[v] == e for v in range(last + 1))
                if n:
                    eng.wait_ge(turn_out[e], n)
            if t == 0:
                eng.wait_ge(hot_out, NO)

        def take_turn(eng, copy, x):
            u = TURNS.index(x)
            s0, s1 = BATCHES[x[1]][x[2]]
            eng.wait_ge(turn_done, u + 1)
            src = turn_ps[u % NBANK][:, 0:(s1 - s0) * P].rearrange("p (s j q) -> p j q s", s=s1 - s0, j=NJ)
            first = TURN_SLOTS[s0]
            dst = embT[:, x[1], :, :, first:first + s1 - s0].rearrange("p q j s -> p j q s")
            copy(dst, src).then_inc(turn_out[TAKERS[u]], 1)

        def hot_bank(i):
            return gram_ps[(NO - i) % 2][:, 0:TB, :].rearrange("p g c -> p (g c)")

        def take_gram(eng, copy, t, h, quadrants, who):
            eng.wait_ge(gram_done, NPART * t + h + 1)
            if h == 0 and t >= 2:
                eng.wait_ge(l1_done, C1 * (t - 1))
            for j in quadrants:
                own = gram_ps[h % 2][FP * j:FP * (j + 1), :, FP * j:FP * (j + 1)]\
                    .rearrange("p q (w b a) -> p w b q a", w=2, a=4)
                for a in range(4):
                    nb = NBLK + (a < 2)
                    last = copy(z_sb[FP * a:FP * (a + 1), t % 2, :, 0:nb, j, GH * h:GH * (h + 1)],
                                own[:, :, 0:nb, :, a])
            last.then_inc(gram_out[who], 1)

        def merge(dve, t, m0, m1):
            for e in ("act", "dve"):
                dve.wait_ge(gram_out[e], NPART * t + m1)
            if t == 0 and m0 == 0:
                dve.wait_ge(other_ready, 1)
            part = z_sb[:, t % 2, :, :, :, m0 * GH:m1 * GH]
            n = (m1 - m0) * GH
            nc.vector.copy_predicated(part[:, 0, 1:NBLK], other[:, 1:NBLK, :, 0:n], part[:, 1, 1:NBLK])\
                .then_inc(z_rest_ready, m1 - m0)
            nc.vector.copy_predicated(part[:, 0, 0], other[:, 0, :, 0:n], part[:, 1, 0]).then_inc(merged, m1 - m0)
            dve.wait_ge(merged, NPART * t + m1)
            nc.vector.copy_predicated(part[0:2 * FP, 0, 0], corner[0:2 * FP, :, 0:n], part[0:2 * FP, 0, NBLK])\
                .then_inc(z0_ready, m1 - m0)

        def place_masks(dve):
            dve.wait_ge(place_set, 1)
            for a in range(4):
                quad = slice(FP * a, FP * (a + 1))
                nc.vector.tensor_scalar(far[quad], place_i[quad, 0:NBLK], float(-FP * a - a - HALF // 2), None,
                                        ALU.add).then_inc(place_ready, 1)
                nc.vector.tensor_scalar(row_no[quad], place_i[quad, 0], float(-FP * a), None, ALU.add)\
                    .then_inc(place_ready, 1)
            dve.wait_ge(place_ready, 8)
            nc.vector.tensor_tensor(far[:], far[:], far[:], ALU.mult).then_inc(place_ready, 1)
            nc.vector.tensor_scalar(main_row[:], row_no[:, 0, 0:1], NF + 1.5, None, ALU.is_lt)\
                .then_inc(place_ready, 1)
            nc.vector.tensor_scalar(corner[:], row_no[:], NF + 2.5, None, ALU.is_gt)
            dve.wait_ge(place_ready, 10)
            nc.vector.tensor_scalar(other[:], far[:], float((HALF // 2 - 1) ** 2) + 0.5, main_row[:, 0:1],
                                    ALU.is_gt, ALU.mult).then_inc(other_ready, 1)

        def relu(eng, who, out, src, bias):
            if who == "act":
                return nc.scalar.activation(out, src, ACT.Relu, bias=bias)
            return nc.vector.tensor_scalar(out, src, bias, 0.0, ALU.add, ALU.max)

        def layer1_out(eng, who, t):
            if t == 0:
                eng.wait_ge(bias_in, 32)
            for c in [c for c in range(C1) if h1_taker(t, c) == who]:
                eng.wait_ge(l1_done, C1 * t + h1_shared(t, c))
                relu(eng, who, h1_sb[:, c, :], h1_ps(t, c), b1_sb[:, c:c + 1]).then_inc(h1_ready[who], 1)

        def layer2_out(eng, who, t):
            m, done = (0, h2_act) if who == "act" else (1, h2_dve)
            eng.wait_ge(l2_done, 2 * t + 1 + m)
            relu(eng, who, h2_sb[:, m, :], h2_ps[m], b2_sb[:, m:m + 1]).then_inc(done, 1)

        @block.sync
        def _(sp):
            def load_table(i):
                if i >= NTBL:
                    sp.wait_ge(lower_ready, OR // FIRST * (i - NTBL + 1))
                f = LOOKUPS[i][0]
                sp.dma_start(ids_bc[:, i % NTBL, 0, :], ids_t[f:f + 1, :].to_broadcast([P, B]))\
                  .then_inc(idbc_in[i % NTBL], 16)
                table = tbls[f].rearrange("(p r) d -> p r d", r=OR)
                first = 0
                if i == 0:
                    first = FIRST
                    sp.dma_start(tbl_sb[0:OP, 0, 0:first, :], table[:, 0:first, :]).then_inc(first_in, 16)
                sp.dma_start(tbl_sb[0:OP, i % NTBL, first:, :], table[:, first:, :]).then_inc(tbl_in[i % NTBL], 16)

            sp.dma_start(ids_sb[:], ids.rearrange("(p t) f -> p t f", p=P)).then_inc(ids_in, 16)
            load_table(0)
            load_table(1)
            sp.dma_start(emb[:, :, 0, :], bottom.rearrange("(p t) d -> p t d", p=P)).then_inc(bottom_in, 16)
            for i in range(2, NO - 2):
                load_table(i)
            sp.dma_start(w1p_sb[:], w1p).then_inc(w1_in, 16)
            sp.dma_start(w1b_sb[:], w1b).then_inc(w1_in, 16)
            sp.dma_start(w2_sb[:], w2.rearrange("(k p) n -> p k n", p=P)).then_inc(w2_in, 16)
            with nc.allow_non_contiguous_dma(reason="a few hundred bias and W_top3 values"):
                sp.dma_start(b1_sb[:], b1.rearrange("(c p) -> p c", p=P)).then_inc(bias_in, 16)
                sp.dma_start(b2_sb[:], b2.rearrange("(c p) -> p c", p=P)).then_inc(bias_in, 16)
                sp.dma_start(w3_sb[:], w3.rearrange("(c p) o -> p (c o)", p=P)).then_inc(w3_in, 16)
            for i in range(NO - 2, NO):
                load_table(i)

            sp.wait_ge(y_out, T)
            sp.dma_start(out.rearrange("b o -> o b"), y_sb[:]).then_inc(stored, 16)
            sp.wait_ge(stored, 16)

        @block.gpsimd
        def _(pool):
            pool.memset(ident[:], 0.0).then_inc(ident_zero, 1)
            pool.iota(row_i[:], pattern=[[1, OR]], base=0, channel_multiplier=OR).then_inc(const_set, 1)
            pool.iota(place_i[:], pattern=[[-4, NBLK + 1], [0, NJ], [0, MG * GH]], base=0,
                      channel_multiplier=1).then_inc(place_set, 1)
            pool.wait_ge(ident_zero, 1)
            pool.affine_select(out=ident[:], in_=ident[:], compare_op=ALU.not_equal, fill=1.0, base=0,
                               pattern=[[-1, P]], channel_multiplier=1).then_inc(const_set, 1)
            pool.wait_ge(ids_in, 16)
            for t in range(T):
                for n, (s0, s1) in enumerate(BATCHES[t]):
                    for s in range(max(s0, 1), s1):
                        f = GATHER[s - 1]
                        pool.indirect_dma_start(emb[:, t, s, :], None, tbls[f],
                                                bass.IndirectOffsetOnAxis(ids_sb[:, t, f:f + 1], 0))\
                            .then_inc(gathered[t][n], 16)

        @block.scalar
        def _(act):
            def less_one(i):
                a = i % NTBL
                act.wait_ge(idbc_in[a], 16 * (i // NTBL + 1))
                if i >= NTBL:
                    act.wait_ge(hot_ready, OR * (i - NTBL + 1))
                cols = slice(P * LOOKUPS[i][2], B)
                nc.scalar.activation(ids_bc[0:OP, a, 1, cols], ids_bc[0:OP, a, 0, cols], ACT.Copy, bias=-1.0)\
                    .then_inc(less_ready, 1)

            def upper_part(i):
                b, a = i % 2, i % NTBL
                if i >= 2:
                    act.wait_ge(hot_done, i - 1)
                    act.wait_ge(lower_ready, OR // FIRST * (i - 1))
                for r in range(0, OR, FIRST):
                    if i == 0 and r == 0:
                        act.wait_ge(first_in, 16)
                    else:
                        act.wait_ge(tbl_in[a], 16 * (i // NTBL + 1))
                    nc.scalar.copy(upper_sb[0:OP, b, r:r + FIRST], tbl_sb[0:OP, a, r:r + FIRST])\
                        .then_inc(upper_ready, 1)

            less_one(0)
            upper_part(0)
            less_one(1)
            for x in STEPS:
                if x[0] == "hot":
                    i = x[1]
                    if i + 1 < NO:
                        upper_part(i + 1)
                    if i + 2 < NO:
                        less_one(i + 2)
                    act.wait_ge(hot_done, i + 1)
                    _, slot, t0 = LOOKUPS[i]
                    for tiles in ([slice(t0, T)] if i < NO - 1 else [slice(0, 1), slice(1, T)]):
                        for row in [n for n in range(FP) if ROWS[n] == slot]:
                            last = nc.scalar.copy(
                                embT[:, tiles, :, :, row].rearrange("p t q j -> p t j q"),
                                hot_bank(i).rearrange("p (t j q) -> p t j q", t=T, j=NJ)[:, tiles])
                        last.then_inc(hot_out, 1)
                elif x[0] == "turn" and TAKERS[TURNS.index(x)] == "act":
                    take_turn(act, nc.scalar.copy, x)
                elif x[0] == "gram":
                    take_gram(act, nc.scalar.copy, x[1], x[2], (2, 3), "act")
                elif x[0] == "l1":
                    layer1_out(act, "act", x[1])
                elif x[0] == "l2":
                    layer2_out(act, "act", x[1])
                elif x[0] == "l3":
                    t = x[1]
                    act.wait_ge(l3_done, t + 1)
                    nc.scalar.copy(y_sb[:].rearrange("o (p t) -> o p t", t=T)[:, :, t], y_ps).then_inc(y_out, 1)

        @block.vector
        def _(dve):
            nc.vector.memset(warm_sb[:], 0.0).then_inc(warm_ready, 1)
            dve.wait_ge(const_set, 2)
            nc.vector.tensor_copy(row_f[:], row_i[:]).then_inc(row_ready, 1)
            dve.wait_ge(row_ready, 1)
            for i in range(NO):
                b, a = i % 2, i % NTBL
                dve.wait_ge(idbc_in[a], 16 * (i // NTBL + 1))
                if i >= 2:
                    dve.wait_ge(hot_done, i - 1)
                cols = slice(P * LOOKUPS[i][2], B)
                single = FIRST if i == 0 else 0
                for r in range(single):
                    nc.vector.tensor_scalar(hot[0:OP, b, r, cols], ids_bc[0:OP, a, 0, cols], row_f[0:OP, r:r + 1],
                                            None, ALU.is_equal).then_inc(hot_ready, 1)
                dve.wait_ge(less_ready, i + 1)
                for r in range(single, OR, 2):
                    nc.vector.tensor_scalar(hot[0:OP, b, r:r + 2, cols], ids_bc[0:OP, a, :, cols],
                                            row_f[0:OP, r:r + 1], None, ALU.is_equal).then_inc(hot_ready, 2)
                dve.wait_ge(upper_ready, OR // FIRST * (i + 1))
                step = FIRST if i < 2 else OR
                for r in range(0, OR, step):
                    nc.vector.tensor_tensor(lower_sb[0:OP, b, r:r + step], tbl_sb[0:OP, a, r:r + step],
                                            upper_sb[0:OP, b, r:r + step].bitcast(fp32),
                                            ALU.subtract).then_inc(lower_ready, step // FIRST)
            place_masks(dve)
            for x in STEPS:
                if x[0] == "turn" and TAKERS[TURNS.index(x)] == "dve":
                    take_turn(dve, nc.vector.tensor_copy, x)
                elif x[0] == "gram":
                    t = x[1]
                    take_gram(dve, nc.vector.tensor_copy, t, x[2], (0, 1), "dve")
                    for m0, m1 in MERGES[t][x[2]]:
                        merge(dve, t, m0, m1)
                elif x[0] == "l1":
                    layer1_out(dve, "dve", x[1])
                elif x[0] == "l2":
                    layer2_out(dve, "dve", x[1])

        @block.tensor
        def _(pe):
            pe.wait_ge(warm_ready, 1)
            for _ in range(WARM):
                nc.tensor.matmul(turn_ps[0][:], warm_sb[:, 0:P], warm_sb[:], start=True, stop=True)

            def hot_table(i):
                b, bank, cols = i % 2, hot_bank(i), slice(P * LOOKUPS[i][2], B)
                if i >= 2:
                    pe.wait_ge(hot_out, i - 1)
                for r in range(OR):
                    if r % FIRST == 0:
                        pe.wait_ge(upper_ready, OR // FIRST * i + r // FIRST + 1)
                    pe.wait_ge(hot_ready, OR * i + r + 1)
                    nc.tensor.matmul(bank[:, cols], upper_sb[0:OP, b, r, :], hot[0:OP, b, r, cols],
                                     start=(r == 0), stop=False)
                for r in range(OR):
                    if r % FIRST == 0:
                        pe.wait_ge(lower_ready, OR // FIRST * i + r // FIRST + 1)
                    last = nc.tensor.matmul(bank[:, cols], lower_sb[0:OP, b, r, :], hot[0:OP, b, r, cols],
                                            start=False, stop=(r == OR - 1))
                last.then_inc(hot_done, 1)

            def transposes(t, n):
                s0, s1 = BATCHES[t][n]
                u = TURNS.index(("turn", t, n))
                if n == 0 and t == 0:
                    pe.wait_ge(bottom_in, 16)
                    pe.wait_ge(const_set, 2)
                pe.wait_ge(gathered[t][n], 16 * (s1 - max(s0, 1)))
                if u >= NBANK:
                    wait_turned(pe, u - NBANK)
                for s in range(s0, s1):
                    last = nc.tensor.transpose(turn_ps[u % NBANK][:, (s - s0) * P:(s - s0 + 1) * P],
                                               emb[:, t, s, :], ident[:])
                last.then_inc(turn_done, 1)

            def gram(t, h):
                if h == 0:
                    wait_features(pe, t)
                if t == 0 and h == 1:
                    pe.wait_ge(hot_out, NO + 1)
                n = NPART * t + h
                if n >= 2:
                    for who in ("act", "dve"):
                        pe.wait_ge(gram_out[who], n - 1)
                for q in range(GH * h, GH * (h + 1)):
                    own = embT[:, t, q, :, :]
                    moving = bass.AP(own.tensor, own.offset, [own.ap[0], [FP, NJ], [HALF, 2], [1, 16]])
                    last = nc.tensor.matmul(
                        gram_ps[h % 2][:, q % GH, :].rearrange("p (j w s) -> p j w s", j=NJ, w=2),
                        own.rearrange("p j s -> p (j s)"), moving, start=True, stop=True)
                last.then_inc(gram_done, 1)

            def layer1(t):
                if t == 0:
                    pe.wait_ge(w1_in, 32)
                else:
                    pe.wait_ge(y_out, t)
                for c in range(C1):
                    nc.tensor.matmul(h1_ps(t, c).rearrange("p (j q) -> p j q", j=NJ),
                                     w1b_sb[:, c * P:(c + 1) * P],
                                     embT[:, t, :, :, 0].rearrange("p q j -> p j q"),
                                     start=(t == T - 1 or c % 2 == 0), stop=False, skip_group_check=True)
                pe.wait_ge(z_rest_ready, NPART * (t + 1))
                for c in range(C1):
                    for b in (*range(1, NBLK), 0):
                        if c == 0 and b == 0:
                            pe.wait_ge(z0_ready, NPART * (t + 1))
                        last = nc.tensor.matmul(h1_ps(t, c), w1p_sb[:, b, c * P:(c + 1) * P],
                                                z_sb[:, t % 2, 0, b, :, :].rearrange("p j q -> p (j q)"),
                                                start=False, stop=(b == 0), skip_group_check=True)
                    last.then_inc(l1_done, 1)

            def layer2(t):
                if t == 0:
                    pe.wait_ge(w2_in, 16)
                for m in range(C2):
                    for c in range(C1):
                        if m == 0:
                            who = h1_taker(t, c)
                            n = [h1_taker(t, i) for i in range(h1_shared(t, c))].count(who)
                            pe.wait_ge(h1_ready[who], C1 // 2 * t + n)
                        last = nc.tensor.matmul(h2_ps[m], w2_sb[:, c, m * P:(m + 1) * P], h1_sb[:, c, :],
                                                start=(c == 0), stop=(c == C1 - 1))
                    last.then_inc(l2_done, 1)

            def layer3(t):
                if t == 0:
                    pe.wait_ge(w3_in, 16)
                for m, ready in enumerate((h2_act, h2_dve)):
                    pe.wait_ge(ready, t + 1)
                    last = nc.tensor.matmul(y_ps, w3_sb[:, m:m + 1], h2_sb[:, m, :],
                                            start=(m == 0), stop=(m == C2 - 1))
                last.then_inc(l3_done, 1)

            for x in STEPS:
                if x[0] == "hot":
                    hot_table(x[1])
                elif x[0] == "turn":
                    transposes(x[1], x[2])
                elif x[0] == "gram":
                    gram(x[1], x[2])
                elif x[0] == "l1":
                    layer1(x[1])
                elif x[0] == "l2":
                    layer2(x[1])
                else:
                    layer3(x[1])


_TABLES = [f"tbl_{f}" for f in range(26)]


def kernel(**inputs):
    import numpy as _np
    import concourse.bacc as _bacc
    from concourse import mybir as _mybir
    from concourse.bass_utils import run_bass_kernel_spmd as _run

    nc = _bacc.Bacc("TRN2", target_bir_lowering=False, num_devices=1)
    pairs = NF * (NF - 1) // 2
    w1 = _np.asarray(inputs["W_top1"])
    ids = _np.asarray(inputs["ids"])
    w1_pairs = _np.zeros((P, NBLK, H1), w1.dtype)
    for part, block, row in pair_place():
        w1_pairs[part, block] = w1[row]
    laid = {
        "r_bottom_output": inputs["r_bottom_output"],
        "ids": ids,
        "ids_t": ids.T.reshape(26, P, T).transpose(0, 2, 1).reshape(26, B),
        **{name: inputs[name] for name in _TABLES},
        "w1_pairs": w1_pairs,
        "w1_bottom": w1[pairs:],
        "b_top1": inputs["b_top1"], "W_top2": inputs["W_top2"], "b_top2": inputs["b_top2"],
        "W_top3": inputs["W_top3"],
    }
    arrays, aps = {}, {}
    for name, a in laid.items():
        a = _np.ascontiguousarray(a)
        arrays[f"in_{name}_dram"] = a
        aps[name] = nc.dram_tensor(f"in_{name}_dram", a.shape, _mybir.dt.from_np(a.dtype),
                                   kind="ExternalInput").ap()
    out = nc.dram_tensor("out_0_dram", (B, 1), _mybir.dt.float32, kind="ExternalOutput").ap()
    tower(nc, aps["r_bottom_output"], aps["ids"], aps["ids_t"], [aps[n] for n in _TABLES],
          aps["w1_pairs"], aps["w1_bottom"], aps["b_top1"], aps["W_top2"], aps["b_top2"],
          aps["W_top3"], out)
    r = _run(nc, [arrays], core_ids=[0])
    return r.results[0]["out_0_dram"]
```
